# Optimizing a Trainium2 kernel written in Bass

```python
import numpy as np
import jax
import jax.numpy as jnp

def _softmax(x, axis=-1):
    return jax.nn.softmax(x, axis=axis)

def _gelu(x):
    return jax.nn.gelu(x, approximate=True)

def _silu(x):
    return jax.nn.silu(x)

def _sigmoid(x):
    return jax.nn.sigmoid(x)

def _layernorm(x, axis=-1, eps=1e-05):
    m = jnp.mean(x, axis=axis, keepdims=True)
    v = jnp.var(x, axis=axis, keepdims=True)
    return (x - m) / jnp.sqrt(v + eps)

def _scatter_add(tgt, idx, src, axis=0):
    return tgt.at[idx].add(src)

def _segment_sum(src, seg, n):
    return jax.ops.segment_sum(src, seg, n)
kernel_name = 'mk_cond_resid_d1_seqx_r2_9d988c'

def setup_inputs(seed: int=0):
    np.random.seed(seed)
    _w = jnp.asarray

    def _rec_inputs():
        import jax
        import jax.numpy as jnp
        _rk = jax.random.key(seed)
        x = -0.0001546 + 1 * jax.random.normal(jax.random.fold_in(_rk, 1), (32, 512, 512), jnp.float32)
        _lenS = 512 - jax.random.randint(jax.random.fold_in(_rk, 7), (32,), 0, max(1, 512 // 4) + 1, jnp.int32)
        _lenS2 = 512 - jax.random.randint(jax.random.fold_in(_rk, 8), (32,), 0, max(1, 512 // 4) + 1, jnp.int32)
        itok_B_1_98 = jax.random.randint(jax.random.fold_in(_rk, 11), (32,), 1, 99, jnp.int32)
        return (x, itok_B_1_98)
    x, itok_B_1_98 = _rec_inputs()

    def _L0_cond_setup():
        import jax, jax.numpy as jnp
        import numpy as np
        B = 128
        D = 512
        K = 100
        key = jax.random.key(seed)
        kx, kt, ks = jax.random.split(key, 3)
        x = jax.random.normal(kx, (B, D, D), dtype=jnp.float32)
        T = jax.random.normal(kt, (K, D, D), dtype=jnp.float32)
        fwd_steps = jax.random.randint(ks, (B,), 1, K + 1, dtype=jnp.int64)
        return {'x': x, 'fwd_steps': fwd_steps, 'T': T}
    _L0_cond_all = _L0_cond_setup()
    _L0_cond_in = {k: v for k, v in _L0_cond_all.items() if k in ('T',)}
    del _L0_cond_all
    return {'x': x, 'itok_B_1_98': itok_B_1_98, 'L0_cond_T': _L0_cond_in['T']}

def reference(x, itok_B_1_98, L0_cond_T):
    import jax
    import jax.numpy as jnp

    def _L0_cond_ref(x, fwd_steps, T):
        import jax, jax.numpy as jnp
        import numpy as np
        B = 128
        D = 512
        K = 100
        Tb = T[fwd_steps - 1]
        return jnp.einsum('bij,bjk->bik', Tb, x)
    x = x + _L0_cond_ref(x, itok_B_1_98, L0_cond_T)
    return x

_drawn_inputs = setup_inputs


def setup_inputs(seed=0):
    import zlib

    import numpy as np

    out = dict(_drawn_inputs(seed))
    spreads = {}
    factors = {}
    for name, (base, spread) in spreads.items():
        noise = np.random.default_rng([zlib.crc32(name.encode()), seed]).standard_normal(out[name].shape)
        drawn = base * np.exp(spread * noise) if base else spread * noise
        out[name] = jnp.asarray(drawn.astype(out[name].dtype))
    for name, factor in factors.items():
        out[name] = (out[name] * factor).astype(out[name].dtype)
    return out
```

```python
import concourse.bass as bass
from concourse import mybir
from contextlib import ExitStack

P = 128
SLOTS = 4
CUTS = 2


def gathered_matmul_residual(nc: bass.Bass, x: bass.AP, itok: bass.AP, table: bass.AP, out: bass.AP):
    fp32 = mybir.dt.float32
    fp32r = mybir.dt.float32r
    int32 = mybir.dt.int32
    ALU = mybir.AluOpType

    B, D, N = x.shape
    K = table.shape[0]
    TILES = D // P
    LOOPS = B // SLOTS
    assert D % P == 0 and N * 4 <= 2048 and B % SLOTS == 0 and SLOTS % CUTS == 0 and LOOPS > 1

    x_rows = x.rearrange("b (t p) n -> b p t n", p=P)
    out_rows = out.rearrange("b (t p) n -> b p t n", p=P)
    table_rows = table.rearrange("k (t p) n -> k p t n", p=P)

    with ExitStack() as ctx:
        def sb(name, shape, dt):
            return ctx.enter_context(nc.sbuf_tensor(name, shape, dt))

        def sem(name):
            return ctx.enter_context(nc.semaphore(name))

        x_in = [sb(f"x_in{s}", [P, TILES, N], fp32) for s in range(SLOTS)]
        t_in = [sb(f"t_in{s}", [P, TILES, D], fp32) for s in range(SLOTS)]
        y_out = [sb(f"y_out{s}", [P, TILES, N], fp32) for s in range(SLOTS)]
        x_high = [sb(f"x_high{s}", [P, TILES, N], fp32r) for s in range(CUTS)]
        x_low = [sb(f"x_low{s}", [P, TILES, N], fp32r) for s in range(CUTS)]
        tt_high = [sb(f"tt_high{s}", [P, TILES, D], fp32r) for s in range(CUTS)]
        tt_low = [sb(f"tt_low{s}", [P, TILES, D], fp32r) for s in range(CUTS)]
        identity = sb("identity", [P, P], fp32)
        token = sb("token", [1, B], int32)
        shifted = sb("shifted", [1, B], fp32)
        wrap = sb("wrap", [1, B], fp32)
        wrapped = sb("wrapped", [1, B], fp32)
        row = sb("row", [1, B], int32)

        tt_bank = [ctx.enter_context(nc.psum_tensor(f"tt_bank{c}", [P, D], fp32)) for c in range(TILES)]
        y_bank = [ctx.enter_context(nc.psum_tensor(f"y_bank{m}", [P, N], fp32)) for m in range(TILES)]

        token_loaded = sem("token_loaded")
        shifted_ready = sem("shifted_ready")
        wrap_ready = sem("wrap_ready")
        wrapped_ready = sem("wrapped_ready")
        row_ready = sem("row_ready")
        zeros_ready = sem("zeros_ready")
        identity_ready = sem("identity_ready")
        x_loaded = [sem(f"x_loaded{s}") for s in range(SLOTS)]
        t_loaded = [sem(f"t_loaded{s}") for s in range(SLOTS)]
        y_slot_free = [sem(f"y_slot_free{s}") for s in range(SLOTS)]
        transposed = sem("transposed")
        tt_high_ready = sem("tt_high_ready")
        tt_low_ready = sem("tt_low_ready")
        x_high_ready = sem("x_high_ready")
        x_low_ready = sem("x_low_ready")
        product_ready = sem("product_ready")
        y_ready = sem("y_ready")

        block = ctx.enter_context(nc.Block())

        @block.gpsimd
        def _(pool):
            nc.gpsimd.memset(identity[:], 0.0).then_inc(zeros_ready, 1)
            pool.wait_ge(zeros_ready, 1)
            nc.gpsimd.affine_select(out=identity[:], in_=identity[:], compare_op=ALU.not_equal, fill=1.0, base=0,
                                    pattern=[[-1, P]], channel_multiplier=1).then_inc(identity_ready, 1)

        @block.sync
        def _(sp):
            sp.dma_start(token[:], itok.rearrange("(o b) -> o b", o=1)).then_inc(token_loaded, 16)

            def load_x(b, s):
                sp.dma_start(x_in[s][:], x_rows[b]).then_inc(x_loaded[s], 16)

            def load_t(b, s):
                k = sp.value_load(row[0:1, bass.ds(b, 1)], min_val=0, max_val=K - 1)
                sp.dma_start(t_in[s][:], table_rows[k]).then_inc(t_loaded[s], 16)

            def store_y(b, s):
                sp.dma_start(out_rows[b], y_out[s][:]).then_inc(y_slot_free[s], 16)

            load_x(0, 0)
            sp.wait_ge(row_ready, 1)
            load_t(0, 0)
            for s in range(1, SLOTS):
                load_x(s, s)
                load_t(s, s)
            with sp.Fori(0, LOOPS - 1) as g:
                for s in range(SLOTS):
                    r = g * SLOTS + s
                    sp.wait_ge(transposed, (r + 1) * TILES)
                    load_t(r + SLOTS, s)
                    sp.wait_ge(y_ready, TILES + (r + 1) * TILES)
                    store_y(r, s)
                    load_x(r + SLOTS, s)
            for s in range(SLOTS):
                r = (LOOPS - 1) * SLOTS + s
                if r < B - 1:
                    sp.wait_ge(y_ready, TILES + (r + 1) * TILES)
                    store_y(r, s)
            for m in range(TILES):
                sp.wait_ge(y_ready, TILES + (B - 1) * TILES + m + 1)
                sp.dma_start(out_rows[B - 1][:, m, :], y_out[SLOTS - 1][:, m, :]).then_inc(y_slot_free[SLOTS - 1], 16)
            for s in range(SLOTS - 1):
                sp.wait_ge(y_slot_free[s], 16 * (1 + LOOPS))
            sp.wait_ge(y_slot_free[SLOTS - 1], 16 * (LOOPS + TILES))

        @block.tensor
        def _(pe):
            def transpose_tile(c, s):
                for t in range(TILES):
                    last = nc.tensor.transpose(tt_bank[c][:, t * P:(t + 1) * P], t_in[s][:, t, c * P:(c + 1) * P],
                                               identity[:])
                last.then_inc(transposed, 1)

            def multiply_tile(m, cut):
                for c in range(TILES):
                    high = tt_high[cut][:, c, m * P:(m + 1) * P]
                    low = tt_low[cut][:, c, m * P:(m + 1) * P]
                    nc.tensor.matmul(y_bank[m][:], low, x_high[cut][:, c, :], start=(c == 0), stop=False)
                    nc.tensor.matmul(y_bank[m][:], high, x_low[cut][:, c, :], start=False, stop=False)
                    last = nc.tensor.matmul(y_bank[m][:], high, x_high[cut][:, c, :], start=False, stop=(c == TILES - 1))
                last.then_inc(product_ready, 1)

            def round_(g, s, ahead):
                r = g * SLOTS + s
                cut = s % CUTS
                for m in range(TILES):
                    if ahead:
                        if m == 0:
                            pe.wait_ge(t_loaded[(s + 1) % SLOTS], 16 * (g + 1 + (s + 1) // SLOTS))
                        pe.wait_ge(tt_low_ready, r * TILES + m + 1)
                        transpose_tile(m, (s + 1) % SLOTS)
                    if m == 0:
                        pe.wait_ge(tt_low_ready, (r + 1) * TILES)
                        pe.wait_ge(x_low_ready, (r + 1) * TILES)
                    pe.wait_ge(y_ready, TILES + (r - 1) * TILES + m + 1)
                    multiply_tile(m, cut)

            pe.wait_ge(identity_ready, 1)
            pe.wait_ge(t_loaded[0], 16)
            for c in range(TILES):
                transpose_tile(c, 0)
            with pe.Fori(0, LOOPS - 1) as g:
                for s in range(SLOTS):
                    round_(g, s, True)
            for s in range(SLOTS):
                round_(LOOPS - 1, s, s < SLOTS - 1)

        @block.scalar
        def _(act):
            def cut_high(b, c, s, cut):
                act.wait_ge(transposed, b * TILES + c + 1)
                nc.scalar.copy(tt_high[cut][:, c, :], tt_bank[c][:]).then_inc(tt_high_ready, 1)
                nc.scalar.copy(x_high[cut][:, c, :], x_in[s][:, c, :]).then_inc(x_high_ready, 1)

            def cut_batch(g, s):
                act.wait_ge(x_loaded[s], 16 * (g + 1))
                for c in range(TILES):
                    cut_high(g * SLOTS + s, c, s, s % CUTS)

            cut_batch(0, 0)
            with act.Fori(0, LOOPS - 1) as g:
                for s in range(SLOTS):
                    cut_batch(g + (s + 1) // SLOTS, (s + 1) % SLOTS)
            for s in range(1, SLOTS):
                cut_batch(LOOPS - 1, s)

        @block.vector
        def _(dve):
            dve.sem_inc(y_ready, TILES)
            for s in range(SLOTS):
                dve.sem_inc(y_slot_free[s], 16)
            dve.wait_ge(token_loaded, 16)
            nc.vector.tensor_scalar(shifted[:], token[:], -1.0, None, ALU.add).then_inc(shifted_ready, 1)
            dve.wait_ge(shifted_ready, 1)
            nc.vector.tensor_scalar(wrap[:], shifted[:], 0.0, float(K), ALU.is_lt, ALU.mult).then_inc(wrap_ready, 1)
            dve.wait_ge(wrap_ready, 1)
            nc.vector.tensor_tensor(wrapped[:], shifted[:], wrap[:], ALU.add).then_inc(wrapped_ready, 1)
            dve.wait_ge(wrapped_ready, 1)
            nc.vector.tensor_scalar(row[:], wrapped[:], 0.0, float(K - 1), ALU.max, ALU.min).then_inc(row_ready, 1)

            def cut_low(b, c, s, cut):
                dve.wait_ge(tt_high_ready, b * TILES + c + 1)
                nc.vector.tensor_tensor(tt_low[cut][:, c, :], tt_bank[c][:], tt_high[cut][:, c, :].bitcast(fp32),
                                        ALU.subtract).then_inc(tt_low_ready, 1)
                dve.wait_ge(x_high_ready, b * TILES + c + 1)
                nc.vector.tensor_tensor(x_low[cut][:, c, :], x_in[s][:, c, :], x_high[cut][:, c, :].bitcast(fp32),
                                        ALU.subtract).then_inc(x_low_ready, 1)

            def round_(g, s, ahead):
                r = g * SLOTS + s
                dve.wait_ge(y_slot_free[s], 16 * (g + 1))
                for m in range(TILES):
                    if ahead:
                        cut_low(r + 1, m, (s + 1) % SLOTS, (s + 1) % CUTS)
                    dve.wait_ge(product_ready, r * TILES + m + 1)
                    nc.vector.tensor_tensor(y_out[s][:, m, :], y_bank[m][:], x_in[s][:, m, :],
                                            ALU.add).then_inc(y_ready, 1)

            for c in range(TILES):
                cut_low(0, c, 0, 0)
            with dve.Fori(0, LOOPS - 1) as g:
                for s in range(SLOTS):
                    round_(g, s, True)
            for s in range(SLOTS):
                round_(LOOPS - 1, s, s < SLOTS - 1)


_INS = ["x", "itok_B_1_98", "L0_cond_T"]


def kernel(**inputs):
    import numpy as _np
    import concourse.bacc as _bacc
    from concourse import mybir as _mybir
    from concourse.bass_utils import run_bass_kernel_spmd as _run

    nc = _bacc.Bacc("TRN2", target_bir_lowering=False, num_devices=1)
    arrays, args = {}, []
    for name in _INS:
        a = _np.ascontiguousarray(inputs[name])
        arrays[f"in_{name}"] = a
        args.append(nc.dram_tensor(f"in_{name}", a.shape, _mybir.dt.from_np(a.dtype), kind="ExternalInput").ap())
    out = nc.dram_tensor("out", inputs["x"].shape, _mybir.dt.float32, kind="ExternalOutput").ap()
    gathered_matmul_residual(nc, *args, out)
    return _run(nc, [arrays], core_ids=[0]).results[0]["out"]
```

```python
import concourse.bass as bass
from concourse import mybir
from contextlib import ExitStack

P = 128
BLOCK = 32
QUADS = P // BLOCK
SLOTS = 4
CUTS = 2
PAIR = 2
SP_QUADS, ACT_QUADS = (0, 1), (2, 3)


def gathered_matmul_residual(nc: bass.Bass, x: bass.AP, itok: bass.AP, table: bass.AP, out: bass.AP):
    fp32 = mybir.dt.float32
    fp32r = mybir.dt.float32r
    int32 = mybir.dt.int32
    ALU = mybir.AluOpType

    B, D, N = x.shape
    K = table.shape[0]
    TILES = D // P
    PAIRS = TILES // PAIR
    ROWS = D // BLOCK
    COLS = D // QUADS
    LOOPS = B // SLOTS
    LOADED = 16 * QUADS
    assert D % P == 0 and N * 4 == 2048 and TILES == QUADS and B % SLOTS == 0 and SLOTS % CUTS == 0 and LOOPS > 1

    x_quads = x.rearrange("b (a c r) n -> b a r c n", a=QUADS, r=BLOCK)
    out_quads = out.rearrange("b (a c r) n -> b a r c n", a=QUADS, r=BLOCK)
    table_quads = table.rearrange("k (i s) (a j) -> k a s i j", s=BLOCK, a=QUADS)

    with ExitStack() as ctx:
        def sb(name, shape, dt):
            return ctx.enter_context(nc.sbuf_tensor(name, shape, dt))

        def sem(name):
            return ctx.enter_context(nc.semaphore(name))

        x_in = [sb(f"x_in{s}", [P, TILES, N], fp32) for s in range(SLOTS)]
        t_in = [sb(f"t_in{s}", [P, ROWS, COLS], fp32) for s in range(SLOTS)]
        y_out = [sb(f"y_out{s}", [P, TILES, N], fp32) for s in range(SLOTS)]
        t_t = sb("t_t", [P, TILES, D], fp32)
        x_high = [sb(f"x_high{s}", [P, TILES, N], fp32r) for s in range(CUTS)]
        x_low = [sb(f"x_low{s}", [P, TILES, N], fp32r) for s in range(CUTS)]
        t_high = [sb(f"t_high{s}", [P, TILES, D], fp32r) for s in range(CUTS)]
        t_low = [sb(f"t_low{s}", [P, TILES, D], fp32r) for s in range(CUTS)]
        token = sb("token", [1, B], int32)
        shifted = sb("shifted", [1, B], fp32)
        wrap = sb("wrap", [1, B], fp32)
        wrapped = sb("wrapped", [1, B], fp32)
        row = sb("row", [1, B], int32)
        y_sum = [ctx.enter_context(nc.psum_tensor(f"y_sum{s}", [P, TILES, N], fp32)) for s in range(CUTS)]

        token_loaded = sem("token_loaded")
        shifted_ready = sem("shifted_ready")
        wrap_ready = sem("wrap_ready")
        wrapped_ready = sem("wrapped_ready")
        row_ready = sem("row_ready")
        x_loaded = [sem(f"x_loaded{s}") for s in range(SLOTS)]
        t_loaded = [sem(f"t_loaded{s}") for s in range(SLOTS)]
        y_stored = [sem(f"y_stored{s}") for s in range(SLOTS)]
        t_t_ready = sem("t_t_ready")
        t_high_ready = sem("t_high_ready")
        t_low_ready = sem("t_low_ready")
        x_high_ready = sem("x_high_ready")
        x_low_ready = sem("x_low_ready")
        product_ready = sem("product_ready")
        y_ready = sem("y_ready")

        block = ctx.enter_context(nc.Block())

        def load_x(queue, quads, b, s):
            for a in quads:
                queue.dma_start(x_in[s][a * BLOCK:(a + 1) * BLOCK], x_quads[b, a]).then_inc(x_loaded[s], 16)

        def load_t(queue, quads, b, s):
            k = queue.value_load(row[0:1, bass.ds(b, 1)], min_val=0, max_val=K - 1)
            for a in quads:
                queue.dma_start(t_in[s][a * BLOCK:(a + 1) * BLOCK], table_quads[k, a]).then_inc(t_loaded[s], 16)

        def store_y(queue, quads, b, s):
            for a in quads:
                queue.dma_start(out_quads[b, a], y_out[s][a * BLOCK:(a + 1) * BLOCK]).then_inc(y_stored[s], 16)

        def first_loads(queue, quads):
            load_x(queue, quads, 0, 0)
            queue.wait_ge(row_ready, 1)
            load_t(queue, quads, 0, 0)
            for s in range(1, SLOTS):
                load_x(queue, quads, s, s)
                load_t(queue, quads, s, s)

        def reload_t(queue, quads, r, s):
            queue.wait_ge(t_t_ready, (r + 1) * PAIRS)
            load_t(queue, quads, r + SLOTS, s)

        def store_and_reload_x(queue, quads, r, s, reload):
            queue.wait_ge(y_ready, (r + 1 + CUTS) * TILES)
            store_y(queue, quads, r, s)
            if reload:
                load_x(queue, quads, r + SLOTS, s)

        def store_last(queue, quads):
            for m in range(TILES):
                queue.wait_ge(y_ready, (B - 1 + CUTS) * TILES + m + 1)
                for a in quads:
                    queue.dma_start(out_quads[B - 1, a][:, m], y_out[SLOTS - 1][a * BLOCK:(a + 1) * BLOCK, m]
                                    ).then_inc(y_stored[SLOTS - 1], 16)

        @block.sync
        def _(sp):
            sp.dma_start(token[:], itok.rearrange("(o b) -> o b", o=1)).then_inc(token_loaded, 16)
            first_loads(sp, SP_QUADS)
            with sp.Fori(0, LOOPS - 1) as g:
                for s in range(SLOTS):
                    reload_t(sp, SP_QUADS, g * SLOTS + s, s)
                    store_and_reload_x(sp, SP_QUADS, g * SLOTS + s, s, True)
            for s in range(SLOTS - 1):
                store_and_reload_x(sp, SP_QUADS, B - SLOTS + s, s, False)
            store_last(sp, SP_QUADS)
            for s in range(SLOTS - 1):
                sp.wait_ge(y_stored[s], LOADED * (1 + LOOPS))
            sp.wait_ge(y_stored[SLOTS - 1], LOADED * (LOOPS + TILES))

        @block.tensor
        def _(pe):
            def multiply(m, c, cut):
                low, high = [t[cut][:, c, m * P:(m + 1) * P] for t in (t_low, t_high)]
                bank = y_sum[cut][:, m]
                nc.tensor.matmul(bank, low, x_high[cut][:, c], start=(c == 0), stop=False)
                nc.tensor.matmul(bank, high, x_low[cut][:, c], start=False, stop=False)
                return nc.tensor.matmul(bank, high, x_high[cut][:, c], start=False, stop=(c == TILES - 1))

            def multiply_batch(r, cut):
                for c in range(TILES):
                    if c % PAIR == 0:
                        pe.wait_ge(t_low_ready, r * PAIRS + c // PAIR + 1)
                        pe.wait_ge(x_low_ready, r * PAIRS + c // PAIR + 1)
                    for m in range(TILES):
                        if c == 0 and m % PAIR == 0:
                            pe.wait_ge(y_ready, r * TILES + m + PAIR)
                        last = multiply(m, c, cut)
                        if c == TILES - 1:
                            last.then_inc(product_ready, 1)

            with pe.Fori(0, LOOPS - 1) as g:
                for s in range(SLOTS):
                    multiply_batch(g * SLOTS + s, s % CUTS)
            for s in range(SLOTS - 1):
                multiply_batch(B - SLOTS + s, s % CUTS)
            pe.wait_ge(t_low_ready, B * PAIRS)
            pe.wait_ge(x_low_ready, B * PAIRS)
            pe.wait_ge(y_ready, B * TILES)
            for m in range(TILES):
                for c in range(TILES):
                    last = multiply(m, c, (B - 1) % CUTS)
                last.then_inc(product_ready, 1)

        @block.scalar
        def _(act):
            def cut_high(g, s):
                for h in range(PAIRS):
                    tiles = slice(h * PAIR, (h + 1) * PAIR)
                    act.wait_ge(t_t_ready, (g * SLOTS + s) * PAIRS + h + 1)
                    nc.scalar.copy(t_high[s % CUTS][:, tiles], t_t[:, tiles]).then_inc(t_high_ready, 1)
                    if h == 0:
                        act.wait_ge(x_loaded[s], LOADED * (g + 1))
                    nc.scalar.copy(x_high[s % CUTS][:, tiles], x_in[s][:, tiles]).then_inc(x_high_ready, 1)

            def cut_high_over(r, g, s):
                act.wait_ge(product_ready, (r + 1) * TILES)
                cut_high(g, s)

            first_loads(act, ACT_QUADS)
            for s in range(CUTS):
                cut_high(0, s)
            with act.Fori(0, LOOPS - 1) as g:
                for s in range(SLOTS):
                    r = g * SLOTS + s
                    reload_t(act, ACT_QUADS, r, s)
                    cut_high_over(r, g + (s + CUTS) // SLOTS, (s + CUTS) % SLOTS)
                    store_and_reload_x(act, ACT_QUADS, r, s, True)
            for s in range(SLOTS - 1):
                if s + CUTS < SLOTS:
                    cut_high_over(B - SLOTS + s, LOOPS - 1, s + CUTS)
                store_and_reload_x(act, ACT_QUADS, B - SLOTS + s, s, False)
            store_last(act, ACT_QUADS)

        @block.gpsimd
        def _(pool):
            def cut_low_x(b, s):
                for h in range(PAIRS):
                    tiles = slice(h * PAIR, (h + 1) * PAIR)
                    pool.wait_ge(x_high_ready, b * PAIRS + h + 1)
                    nc.gpsimd.tensor_tensor(x_low[s % CUTS][:, tiles], x_in[s][:, tiles],
                                            x_high[s % CUTS][:, tiles].bitcast(fp32), ALU.subtract).then_inc(x_low_ready, 1)

            with pool.Fori(0, LOOPS) as g:
                for s in range(SLOTS):
                    cut_low_x(g * SLOTS + s, s)

        @block.vector
        def _(dve):
            dve.sem_inc(y_ready, CUTS * TILES)
            for s in range(SLOTS):
                dve.sem_inc(y_stored[s], LOADED)
            dve.wait_ge(token_loaded, 16)
            nc.vector.tensor_scalar(shifted[:], token[:], -1.0, None, ALU.add).then_inc(shifted_ready, 1)
            dve.wait_ge(shifted_ready, 1)
            nc.vector.tensor_scalar(wrap[:], shifted[:], 0.0, float(K), ALU.is_lt, ALU.mult).then_inc(wrap_ready, 1)
            dve.wait_ge(wrap_ready, 1)
            nc.vector.tensor_tensor(wrapped[:], shifted[:], wrap[:], ALU.add).then_inc(wrapped_ready, 1)
            dve.wait_ge(wrapped_ready, 1)
            nc.vector.tensor_scalar(row[:], wrapped[:], 0.0, float(K - 1), ALU.max, ALU.min).then_inc(row_ready, 1)

            def transpose(b, s, h, overwrites=True):
                if overwrites:
                    dve.wait_ge(t_low_ready, (b - 1) * PAIRS + h + 1)
                for c in range(h * PAIR, (h + 1) * PAIR):
                    last = nc.vector.transpose(
                        t_t[:, c].rearrange("p (m a s) -> p a m s", a=QUADS, s=BLOCK),
                        t_in[s][:, :, c * BLOCK:(c + 1) * BLOCK].rearrange("p (a m) r -> p a m r", a=QUADS))
                last.then_inc(t_t_ready, 1)

            def cut_low_t(b, s, h):
                tiles = slice(h * PAIR, (h + 1) * PAIR)
                dve.wait_ge(t_high_ready, b * PAIRS + h + 1)
                nc.vector.tensor_tensor(t_low[s % CUTS][:, tiles], t_t[:, tiles],
                                        t_high[s % CUTS][:, tiles].bitcast(fp32), ALU.subtract).then_inc(t_low_ready, 1)

            def add_x(r, s, m, tiles):
                dve.wait_ge(product_ready, r * TILES + m + tiles)
                nc.vector.tensor_tensor(y_out[s][:, m:m + tiles], y_sum[s % CUTS][:, m:m + tiles],
                                        x_in[s][:, m:m + tiles], ALU.add).then_inc(y_ready, tiles)

            def step(g, s, ahead):
                r = g * SLOTS + s
                b, b_g, b_s = r + CUTS, g + (s + CUTS) // SLOTS, (s + CUTS) % SLOTS
                if ahead:
                    dve.wait_ge(t_loaded[b_s], LOADED * (b_g + 1))
                for h in range(PAIRS):
                    if ahead:
                        transpose(b, b_s, h)
                    if h == 0:
                        dve.wait_ge(y_stored[s], LOADED * (g + 1))
                    add_x(r, s, h * PAIR, PAIR)
                    if ahead:
                        cut_low_t(b, b_s, h)

            for s in range(CUTS):
                dve.wait_ge(t_loaded[s], LOADED)
                for h in range(PAIRS):
                    transpose(s, s, h, overwrites=s > 0)
                for h in range(PAIRS):
                    cut_low_t(s, s, h)
            with dve.Fori(0, LOOPS - 1) as g:
                for s in range(SLOTS):
                    step(g, s, True)
            for s in range(SLOTS - 1):
                step(LOOPS - 1, s, s + CUTS < SLOTS)
            dve.wait_ge(y_stored[SLOTS - 1], LOADED * LOOPS)
            for m in range(TILES):
                add_x(B - 1, SLOTS - 1, m, 1)


_INS = ["x", "itok_B_1_98", "L0_cond_T"]


def kernel(**inputs):
    import numpy as _np
    import concourse.bacc as _bacc
    from concourse import mybir as _mybir
    from concourse.bass_utils import run_bass_kernel_spmd as _run

    nc = _bacc.Bacc("TRN2", target_bir_lowering=False, num_devices=1)
    arrays, args = {}, []
    for name in _INS:
        a = _np.ascontiguousarray(inputs[name])
        arrays[f"in_{name}"] = a
        args.append(nc.dram_tensor(f"in_{name}", a.shape, _mybir.dt.from_np(a.dtype), kind="ExternalInput").ap())
    out = nc.dram_tensor("out", inputs["x"].shape, _mybir.dt.float32, kind="ExternalOutput").ap()
    gathered_matmul_residual(nc, *args, out)
    return _run(nc, [arrays], core_ids=[0]).results[0]["out"]
```

```python
import concourse.bass as bass
from concourse import mybir
from contextlib import ExitStack

P = 128
BLOCK = 32
QUADS = P // BLOCK
SLOTS = 4
CUTS = 2
PAIR = 2
SP_QUADS, ACT_QUADS = (0, 1), (2, 3)


def gathered_matmul_residual(nc: bass.Bass, x: bass.AP, itok: bass.AP, table: bass.AP, out: bass.AP):
    fp32 = mybir.dt.float32
    fp32r = mybir.dt.float32r
    int32 = mybir.dt.int32
    ALU = mybir.AluOpType

    B, D, N = x.shape
    K = table.shape[0]
    TILES = D // P
    ROWS = D // BLOCK
    COLS = D // QUADS
    LOOPS = B // SLOTS
    LOADED = 16 * QUADS
    assert D % P == 0 and N * 4 == 2048 and TILES == QUADS and B % SLOTS == 0 and SLOTS % CUTS == 0 and LOOPS > 1

    x_quads = x.rearrange("b (a c r) n -> b a r c n", a=QUADS, r=BLOCK)
    out_quads = out.rearrange("b (a c r) n -> b a r c n", a=QUADS, r=BLOCK)
    table_quads = table.rearrange("k (i s) (a j) -> k a s i j", s=BLOCK, a=QUADS)

    with ExitStack() as ctx:
        def sb(name, shape, dt):
            return ctx.enter_context(nc.sbuf_tensor(name, shape, dt))

        def sem(name):
            return ctx.enter_context(nc.semaphore(name))

        x_in = [sb(f"x_in{s}", [P, TILES, N], fp32) for s in range(SLOTS)]
        t_in = [sb(f"t_in{s}", [P, ROWS, COLS], fp32) for s in range(SLOTS)]
        y_out = [sb(f"y_out{s}", [P, TILES, N], fp32) for s in range(SLOTS)]
        t_t = sb("t_t", [P, TILES, D], fp32)
        x_high = [sb(f"x_high{s}", [P, TILES, N], fp32r) for s in range(CUTS)]
        x_low = [sb(f"x_low{s}", [P, TILES, N], fp32r) for s in range(CUTS)]
        t_high = [sb(f"t_high{s}", [P, TILES, D], fp32r) for s in range(CUTS)]
        t_low = [sb(f"t_low{s}", [P, TILES, D], fp32r) for s in range(CUTS)]
        token = sb("token", [1, B], int32)
        shifted = sb("shifted", [1, B], fp32)
        wrap = sb("wrap", [1, B], fp32)
        wrapped = sb("wrapped", [1, B], fp32)
        row = sb("row", [1, B], int32)
        y_sum = [ctx.enter_context(nc.psum_tensor(f"y_sum{s}", [P, TILES, N], fp32)) for s in range(CUTS)]

        token_loaded = sem("token_loaded")
        shifted_ready = sem("shifted_ready")
        wrap_ready = sem("wrap_ready")
        wrapped_ready = sem("wrapped_ready")
        row_ready = sem("row_ready")
        x_loaded = [sem(f"x_loaded{s}") for s in range(SLOTS)]
        t_loaded = [sem(f"t_loaded{s}") for s in range(SLOTS)]
        y_stored = [sem(f"y_stored{s}") for s in range(SLOTS)]
        t_t_ready = sem("t_t_ready")
        t_high_ready = sem("t_high_ready")
        t_low_ready = sem("t_low_ready")
        x_high_ready = sem("x_high_ready")
        x_low_ready = sem("x_low_ready")
        product_ready = sem("product_ready")
        y_ready = sem("y_ready")

        block = ctx.enter_context(nc.Block())

        def matrices_of(queue, g):
            _, matrices = nc.values_load_multi_w_load_instructions(
                row[0:1, bass.ds(g * SLOTS, SLOTS)], engines=(queue.engine,), min_val=0, max_val=K - 1)
            return matrices

        def load_x(queue, quads, b, s):
            for a in quads:
                queue.dma_start(x_in[s][a * BLOCK:(a + 1) * BLOCK], x_quads[b, a]).then_inc(x_loaded[s], 16)

        def load_t(queue, quads, matrix, s):
            for a in quads:
                queue.dma_start(t_in[s][a * BLOCK:(a + 1) * BLOCK], table_quads[matrix, a]).then_inc(t_loaded[s], 16)

        def store_y(queue, quads, b, s):
            for a in quads:
                queue.dma_start(out_quads[b, a], y_out[s][a * BLOCK:(a + 1) * BLOCK]).then_inc(y_stored[s], 16)

        def store_y_tile(queue, quads, b, s, m):
            for a in quads:
                queue.dma_start(out_quads[b, a][:, m], y_out[s][a * BLOCK:(a + 1) * BLOCK, m]).then_inc(y_stored[s], 16)

        @block.sync
        def _(sp):
            sp.dma_start(token[:], itok.rearrange("(o b) -> o b", o=1)).then_inc(token_loaded, 16)
            load_x(sp, SP_QUADS, 0, 0)
            sp.wait_ge(row_ready, 1)
            matrices = matrices_of(sp, 0)
            load_t(sp, SP_QUADS, matrices[0], 0)
            for s in range(1, SLOTS):
                load_t(sp, SP_QUADS, matrices[s], s)
                load_x(sp, SP_QUADS, s, s)
            with sp.Fori(0, LOOPS - 1) as g:
                matrices = matrices_of(sp, g + 1)
                for s in range(SLOTS):
                    r = g * SLOTS + s
                    sp.wait_ge(t_t_ready, (r + 1) * TILES)
                    load_t(sp, SP_QUADS, matrices[s], s)
                    sp.wait_ge(y_ready, (r + 1 + CUTS) * TILES)
                    store_y(sp, SP_QUADS, r, s)
                    load_x(sp, SP_QUADS, r + SLOTS, s)
            for s in range(SLOTS - 1):
                sp.wait_ge(y_ready, (B - SLOTS + s + 1 + CUTS) * TILES)
                store_y(sp, SP_QUADS, B - SLOTS + s, s)
            for m in range(TILES):
                sp.wait_ge(y_ready, (B - 1 + CUTS) * TILES + m + 1)
                store_y_tile(sp, SP_QUADS, B - 1, SLOTS - 1, m)
            for s in range(SLOTS - 1):
                sp.wait_ge(y_stored[s], LOADED * (1 + LOOPS))
            sp.wait_ge(y_stored[SLOTS - 1], LOADED * (LOOPS + TILES))

        @block.tensor
        def _(pe):
            def multiply(m, c, cut):
                low, high = [t[cut][:, c, m * P:(m + 1) * P] for t in (t_low, t_high)]
                bank = y_sum[cut][:, m]
                nc.tensor.matmul(bank, low, x_high[cut][:, c], start=(c == 0), stop=False)
                nc.tensor.matmul(bank, high, x_low[cut][:, c], start=False, stop=False)
                return nc.tensor.matmul(bank, high, x_high[cut][:, c], start=False, stop=(c == TILES - 1))

            def multiply_batch(r, cut):
                for c in range(TILES):
                    pe.wait_ge(t_low_ready, r * TILES + c + 1)
                    if c % PAIR == 0:
                        pe.wait_ge(x_low_ready, r * TILES + c + PAIR)
                    for m in range(TILES):
                        if c == 0 and m % PAIR == 0:
                            pe.wait_ge(y_ready, r * TILES + m + PAIR)
                        last = multiply(m, c, cut)
                        if c == TILES - 1:
                            last.then_inc(product_ready, 1)

            with pe.Fori(0, LOOPS - 1) as g:
                for s in range(SLOTS):
                    multiply_batch(g * SLOTS + s, s % CUTS)
            for s in range(SLOTS - 1):
                multiply_batch(B - SLOTS + s, s % CUTS)
            pe.wait_ge(t_low_ready, B * TILES)
            pe.wait_ge(x_low_ready, B * TILES)
            pe.wait_ge(y_ready, B * TILES)
            for m in range(TILES):
                for c in range(TILES):
                    last = multiply(m, c, (B - 1) % CUTS)
                last.then_inc(product_ready, 1)

        @block.scalar
        def _(act):
            def cut_high_t(b, s, c, tiles):
                act.wait_ge(t_t_ready, b * TILES + c + tiles)
                nc.scalar.copy(t_high[s % CUTS][:, c:c + tiles], t_t[:, c:c + tiles]).then_inc(t_high_ready, tiles)

            def cut_high_x(g, s):
                act.wait_ge(x_loaded[s], LOADED * (g + 1))
                for c in range(0, TILES, PAIR):
                    nc.scalar.copy(x_high[s % CUTS][:, c:c + PAIR], x_in[s][:, c:c + PAIR]).then_inc(x_high_ready, PAIR)

            load_x(act, ACT_QUADS, 0, 0)
            act.wait_ge(row_ready, 1)
            matrices = matrices_of(act, 0)
            load_t(act, ACT_QUADS, matrices[0], 0)
            cut_high_x(0, 0)
            cut_high_t(0, 0, 0, 1)
            load_t(act, ACT_QUADS, matrices[1], 1)
            cut_high_t(0, 0, 1, 1)
            load_x(act, ACT_QUADS, 1, 1)
            for c in range(PAIR, TILES):
                cut_high_t(0, 0, c, 1)
            cut_high_t(1, 1, 0, PAIR)
            cut_high_x(0, 1)
            load_t(act, ACT_QUADS, matrices[2], 2)
            load_x(act, ACT_QUADS, 2, 2)
            cut_high_t(1, 1, PAIR, PAIR)
            load_t(act, ACT_QUADS, matrices[3], 3)
            load_x(act, ACT_QUADS, 3, 3)
            with act.Fori(0, LOOPS - 1) as g:
                matrices = matrices_of(act, g + 1)
                for s in range(SLOTS):
                    r = g * SLOTS + s
                    next_g, next_s = g + (s + CUTS) // SLOTS, (s + CUTS) % SLOTS
                    act.wait_ge(product_ready, (r + 1) * TILES)
                    cut_high_t(r + CUTS, next_s, 0, PAIR)
                    cut_high_x(next_g, next_s)
                    act.wait_ge(t_t_ready, (r + 1) * TILES)
                    load_t(act, ACT_QUADS, matrices[s], s)
                    cut_high_t(r + CUTS, next_s, PAIR, PAIR)
                    act.wait_ge(y_ready, (r + 1 + CUTS) * TILES)
                    store_y(act, ACT_QUADS, r, s)
                    load_x(act, ACT_QUADS, r + SLOTS, s)
            for s in range(SLOTS - 1):
                r = B - SLOTS + s
                if s + CUTS < SLOTS:
                    act.wait_ge(product_ready, (r + 1) * TILES)
                    cut_high_t(r + CUTS, s + CUTS, 0, PAIR)
                    cut_high_x(LOOPS - 1, s + CUTS)
                    cut_high_t(r + CUTS, s + CUTS, PAIR, PAIR)
                act.wait_ge(y_ready, (r + 1 + CUTS) * TILES)
                store_y(act, ACT_QUADS, r, s)
            for m in range(TILES):
                act.wait_ge(y_ready, (B - 1 + CUTS) * TILES + m + 1)
                store_y_tile(act, ACT_QUADS, B - 1, SLOTS - 1, m)

        @block.gpsimd
        def _(pool):
            def cut_low_x(b, s):
                for c in range(0, TILES, PAIR):
                    tiles = slice(c, c + PAIR)
                    pool.wait_ge(x_high_ready, b * TILES + c + PAIR)
                    nc.gpsimd.tensor_tensor(x_low[s % CUTS][:, tiles], x_in[s][:, tiles], x_high[s % CUTS][:, tiles].bitcast(fp32),
                                            ALU.subtract).then_inc(x_low_ready, PAIR)

            with pool.Fori(0, LOOPS) as g:
                for s in range(SLOTS):
                    cut_low_x(g * SLOTS + s, s)

        @block.vector
        def _(dve):
            dve.sem_inc(y_ready, CUTS * TILES)
            for s in range(SLOTS):
                dve.sem_inc(y_stored[s], LOADED)
            dve.wait_ge(token_loaded, 16)
            nc.vector.tensor_scalar(shifted[:], token[:], -1.0, None, ALU.add).then_inc(shifted_ready, 1)
            nc.vector.tensor_scalar(wrap[:], token[:], 1.0, float(K), ALU.is_lt, ALU.mult).then_inc(wrap_ready, 1)
            dve.wait_ge(shifted_ready, 1)
            dve.wait_ge(wrap_ready, 1)
            nc.vector.tensor_tensor(wrapped[:], shifted[:], wrap[:], ALU.add).then_inc(wrapped_ready, 1)
            dve.wait_ge(wrapped_ready, 1)
            nc.vector.tensor_scalar(row[:], wrapped[:], 0.0, float(K - 1), ALU.max, ALU.min).then_inc(row_ready, 1)

            def transpose(b, s, c, tiles, overwrites=True):
                if overwrites:
                    dve.wait_ge(t_low_ready, (b - 1) * TILES + c + tiles)
                for c in range(c, c + tiles):
                    nc.vector.transpose(
                        t_t[:, c].rearrange("p (m a s) -> p a m s", a=QUADS, s=BLOCK),
                        t_in[s][:, :, c * BLOCK:(c + 1) * BLOCK].rearrange("p (a m) r -> p a m r", a=QUADS)
                    ).then_inc(t_t_ready, 1)

            def cut_low_t(b, s, c, tiles):
                dve.wait_ge(t_high_ready, b * TILES + c + tiles)
                nc.vector.tensor_tensor(t_low[s % CUTS][:, c:c + tiles], t_t[:, c:c + tiles],
                                        t_high[s % CUTS][:, c:c + tiles].bitcast(fp32), ALU.subtract
                                        ).then_inc(t_low_ready, tiles)

            def add_x(r, s, m, tiles):
                dve.wait_ge(product_ready, r * TILES + m + tiles)
                nc.vector.tensor_tensor(y_out[s][:, m:m + tiles], y_sum[s % CUTS][:, m:m + tiles],
                                        x_in[s][:, m:m + tiles], ALU.add).then_inc(y_ready, tiles)

            def step(g, s, ahead):
                r = g * SLOTS + s
                b, b_g, b_s = r + CUTS, g + (s + CUTS) // SLOTS, (s + CUTS) % SLOTS
                if ahead:
                    dve.wait_ge(t_loaded[b_s], LOADED * (b_g + 1))
                for c in range(0, TILES, PAIR):
                    if ahead:
                        transpose(b, b_s, c, PAIR)
                    if c == 0:
                        dve.wait_ge(y_stored[s], LOADED * (g + 1))
                    add_x(r, s, c, PAIR)
                    if ahead:
                        cut_low_t(b, b_s, c, PAIR)

            dve.wait_ge(t_loaded[0], LOADED)
            for c in range(TILES):
                transpose(0, 0, c, 1, overwrites=False)
                if c > 0:
                    cut_low_t(0, 0, c - 1, 1)
            cut_low_t(0, 0, TILES - 1, 1)
            dve.wait_ge(t_loaded[1], LOADED)
            for c in range(0, TILES, PAIR):
                transpose(1, 1, c, PAIR)
            for c in range(0, TILES, PAIR):
                cut_low_t(1, 1, c, PAIR)
            with dve.Fori(0, LOOPS - 1) as g:
                for s in range(SLOTS):
                    step(g, s, True)
            for s in range(SLOTS - 1):
                step(LOOPS - 1, s, s + CUTS < SLOTS)
            dve.wait_ge(y_stored[SLOTS - 1], LOADED * LOOPS)
            for m in range(TILES):
                add_x(B - 1, SLOTS - 1, m, 1)


_INS = ["x", "itok_B_1_98", "L0_cond_T"]


def kernel(**inputs):
    import numpy as _np
    import concourse.bacc as _bacc
    from concourse import mybir as _mybir
    from concourse.bass_utils import run_bass_kernel_spmd as _run

    nc = _bacc.Bacc("TRN2", target_bir_lowering=False, num_devices=1)
    arrays, args = {}, []
    for name in _INS:
        a = _np.ascontiguousarray(inputs[name])
        arrays[f"in_{name}"] = a
        args.append(nc.dram_tensor(f"in_{name}", a.shape, _mybir.dt.from_np(a.dtype), kind="ExternalInput").ap())
    out = nc.dram_tensor("out", inputs["x"].shape, _mybir.dt.float32, kind="ExternalOutput").ap()
    gathered_matmul_residual(nc, *args, out)
    return _run(nc, [arrays], core_ids=[0]).results[0]["out"]
```
